# Optimizing a Trainium2 kernel written in Bass

```python
import numpy as np
import jax
import jax.numpy as jnp

def _softmax(x, axis=-1):
    return jax.nn.softmax(x, axis=axis)

def _gelu(x):
    return jax.nn.gelu(x, approximate=True)

def _silu(x):
    return jax.nn.silu(x)

def _sigmoid(x):
    return jax.nn.sigmoid(x)

def _layernorm(x, axis=-1, eps=1e-05):
    m = jnp.mean(x, axis=axis, keepdims=True)
    v = jnp.var(x, axis=axis, keepdims=True)
    return (x - m) / jnp.sqrt(v + eps)

def _scatter_add(tgt, idx, src, axis=0):
    return tgt.at[idx].add(src)

def _segment_sum(src, seg, n):
    return jax.ops.segment_sum(src, seg, n)
kernel_name = 'mk_macaron_d2_jaxref_r8_d9777d'

def setup_inputs(seed: int=0):
    np.random.seed(seed)
    _w = jnp.asarray

    def _L0_attn_setup():
        import jax, jax.numpy as jnp
        import numpy as np
        B, T, D, H = (4, 256, 128, 16)
        HD = D // H
        EPS = 1e-05
        NEG = 10000000000.0
        key = jax.random.key(seed)
        k1, k2, k3 = jax.random.split(key, 3)
        return {'target': jax.random.normal(k1, (B, T, D), dtype=jnp.float32), 'w_qkv': jax.random.normal(k2, (D, 3 * D), dtype=jnp.float32) * 0.02, 'w_proj': jax.random.normal(k3, (D, D), dtype=jnp.float32) * (0.02 / np.sqrt(24.0)), 'b_proj': jnp.zeros((D,), dtype=jnp.float32), 'ln_gamma': jnp.ones((D,), dtype=jnp.float32), 'ln_beta': jnp.zeros((D,), dtype=jnp.float32)}
    _L0_attn_in = _L0_attn_setup()

    def _L0_ffn_setup():
        import jax, jax.numpy as jnp
        import numpy as np
        B, S, DIM = (4, 512, 128)
        BASE_COUPLING = 0.1
        NUM_CYCLES = 3

        def _gelu(x):
            return jax.nn.gelu(x, approximate=False)

        def _coupling_net(h, w1, b1, w2, b2, w3, b3, w4, b4):
            h = _gelu(h @ w1 + b1)
            h = _gelu(h @ w2 + b2)
            h = _gelu(h @ w3 + b3)
            return jax.nn.sigmoid(h @ w4 + b4)

        def _global_net(h, w1, b1, w2, b2, w3, b3):
            h = _gelu(h @ w1 + b1)
            h = _gelu(h @ w2 + b2)
            return jax.nn.sigmoid(h @ w3 + b3)

        def _twist(x):
            o_r, o_i, p_r, p_i = jnp.split(x, 4, axis=-1)
            return jnp.concatenate([p_r, -p_i, -o_r, o_i], axis=-1)
        key = jax.random.key(seed)
        ks = jax.random.split(key, 9)
        d = DIM

        def w(k, fan_in, fan_out):
            return jax.random.normal(k, (fan_in, fan_out), dtype=jnp.float32) / np.sqrt(fan_in).astype(np.float32)
        inp = {'x': jax.random.normal(ks[0], (B, S, d), dtype=jnp.float32)}
        cn_dims = [(d, d), (d, d // 2), (d // 2, d // 4), (d // 4, 1)]
        for i, (a, b) in enumerate(cn_dims):
            inp[f'cn_w{i + 1}'] = w(ks[1 + i], a, b)
            inp[f'cn_b{i + 1}'] = jnp.zeros((b,), dtype=jnp.float32)
        gc_dims = [(d, d // 2), (d // 2, d // 4), (d // 4, 1)]
        for i, (a, b) in enumerate(gc_dims):
            inp[f'gc_w{i + 1}'] = w(ks[5 + i], a, b)
            inp[f'gc_b{i + 1}'] = jnp.zeros((b,), dtype=jnp.float32)
        inp['adaptive_range'] = jnp.full((1,), 0.2, dtype=jnp.float32)
        return inp
    _L0_ffn_in = _L0_ffn_setup()

    def _L1_attn_setup():
        import jax, jax.numpy as jnp
        import numpy as np
        B, N, C = (2, 256, 128)
        H = 16
        HD = C // H
        R = 16
        LORA_SCALE = 32.0 / R
        ATTN_SCALE = HD ** (-0.5)
        key = jax.random.key(seed)
        ks = jax.random.split(key, 10)
        s = lambda fan_in: 1.0 / np.sqrt(fan_in)
        return {'x': jax.random.normal(ks[0], (B, N, C), dtype=jnp.float32), 'w_qkv': jax.random.normal(ks[1], (C, 3 * C), dtype=jnp.float32) * s(C), 'b_qkv': jax.random.normal(ks[2], (3 * C,), dtype=jnp.float32) * 0.02, 'a_q': jax.random.normal(ks[3], (HD, R), dtype=jnp.float32) * s(HD), 'b_q': jax.random.normal(ks[4], (R, HD), dtype=jnp.float32) * 0.02, 'a_v': jax.random.normal(ks[5], (HD, R), dtype=jnp.float32) * s(HD), 'b_v': jax.random.normal(ks[6], (R, HD), dtype=jnp.float32) * 0.02, 'w_proj': jax.random.normal(ks[7], (C, C), dtype=jnp.float32) * s(C), 'b_proj': jax.random.normal(ks[8], (C,), dtype=jnp.float32) * 0.02}
    _L1_attn_in = _L1_attn_setup()

    def _L1_ffn_setup():
        import jax, jax.numpy as jnp
        import numpy as np
        TOP_K = 2
        NUM_EXPERTS = 8
        key = jax.random.key(seed)
        ks = jax.random.split(key, 8)
        h, d, ds, E = (128, 64, 128, NUM_EXPERTS)
        s = 1.0 / np.sqrt(h)
        return {'x': jax.random.normal(ks[0], (2, 256, h), jnp.float32), 'router': jax.random.normal(ks[1], (h, E), jnp.float32) * s, 'experts_gate': jax.random.normal(ks[2], (E, h, d), jnp.float32) * s, 'experts_up': jax.random.normal(ks[3], (E, h, d), jnp.float32) * s, 'experts_down': jax.random.normal(ks[4], (E, d, h), jnp.float32) * (1.0 / np.sqrt(d)), 'shared_gate': jax.random.normal(ks[5], (h, ds), jnp.float32) * s, 'shared_up': jax.random.normal(ks[6], (h, ds), jnp.float32) * s, 'shared_down': jax.random.normal(ks[7], (ds, h), jnp.float32) * (1.0 / np.sqrt(ds))}
    _L1_ffn_in = _L1_ffn_setup()
    _d = {'L0_attn_target': _L0_attn_in['target'], 'L0_attn_w_qkv': _L0_attn_in['w_qkv'], 'L0_attn_w_proj': _L0_attn_in['w_proj'], 'L0_attn_b_proj': _L0_attn_in['b_proj'], 'L0_attn_ln_gamma': _L0_attn_in['ln_gamma'], 'L0_attn_ln_beta': _L0_attn_in['ln_beta'], 'L0_ffn_cn_w1': _L0_ffn_in['cn_w1'], 'L0_ffn_cn_b1': _L0_ffn_in['cn_b1'], 'L0_ffn_cn_w2': _L0_ffn_in['cn_w2'], 'L0_ffn_cn_b2': _L0_ffn_in['cn_b2'], 'L0_ffn_cn_w3': _L0_ffn_in['cn_w3'], 'L0_ffn_cn_b3': _L0_ffn_in['cn_b3'], 'L0_ffn_cn_w4': _L0_ffn_in['cn_w4'], 'L0_ffn_cn_b4': _L0_ffn_in['cn_b4'], 'L0_ffn_gc_w1': _L0_ffn_in['gc_w1'], 'L0_ffn_gc_b1': _L0_ffn_in['gc_b1'], 'L0_ffn_gc_w2': _L0_ffn_in['gc_w2'], 'L0_ffn_gc_b2': _L0_ffn_in['gc_b2'], 'L0_ffn_gc_w3': _L0_ffn_in['gc_w3'], 'L0_ffn_gc_b3': _L0_ffn_in['gc_b3'], 'L0_ffn_adaptive_range': _L0_ffn_in['adaptive_range'], 'L1_attn_w_qkv': _L1_attn_in['w_qkv'], 'L1_attn_b_qkv': _L1_attn_in['b_qkv'], 'L1_attn_a_q': _L1_attn_in['a_q'], 'L1_attn_b_q': _L1_attn_in['b_q'], 'L1_attn_a_v': _L1_attn_in['a_v'], 'L1_attn_b_v': _L1_attn_in['b_v'], 'L1_attn_w_proj': _L1_attn_in['w_proj'], 'L1_attn_b_proj': _L1_attn_in['b_proj'], 'L1_ffn_router': _L1_ffn_in['router'], 'L1_ffn_experts_gate': _L1_ffn_in['experts_gate'], 'L1_ffn_experts_up': _L1_ffn_in['experts_up'], 'L1_ffn_experts_down': _L1_ffn_in['experts_down'], 'L1_ffn_shared_gate': _L1_ffn_in['shared_gate'], 'L1_ffn_shared_up': _L1_ffn_in['shared_up'], 'L1_ffn_shared_down': _L1_ffn_in['shared_down']}
    _x0 = _d['L0_attn_target']
    _d['L0_attn_target'] = jax.random.normal(jax.random.fold_in(jax.random.key(seed), 1), (1, 2048, 128), dtype=_x0.dtype)
    del _x0
    return _d

def reference(L0_attn_target, L0_attn_w_qkv, L0_attn_w_proj, L0_attn_b_proj, L0_attn_ln_gamma, L0_attn_ln_beta, L0_ffn_cn_w1, L0_ffn_cn_b1, L0_ffn_cn_w2, L0_ffn_cn_b2, L0_ffn_cn_w3, L0_ffn_cn_b3, L0_ffn_cn_w4, L0_ffn_cn_b4, L0_ffn_gc_w1, L0_ffn_gc_b1, L0_ffn_gc_w2, L0_ffn_gc_b2, L0_ffn_gc_w3, L0_ffn_gc_b3, L0_ffn_adaptive_range, L1_attn_w_qkv, L1_attn_b_qkv, L1_attn_a_q, L1_attn_b_q, L1_attn_a_v, L1_attn_b_v, L1_attn_w_proj, L1_attn_b_proj, L1_ffn_router, L1_ffn_experts_gate, L1_ffn_experts_up, L1_ffn_experts_down, L1_ffn_shared_gate, L1_ffn_shared_up, L1_ffn_shared_down):

    def _L0_attn_ref(target, w_qkv, w_proj, b_proj, ln_gamma, ln_beta):
        import jax, jax.numpy as jnp
        import numpy as np
        B, T, D, H = (4, 256, 128, 16)
        HD = D // H
        EPS = 1e-05
        NEG = 10000000000.0
        b, t, d = target.shape
        resid = target
        qkv = target @ w_qkv
        q, k, v = jnp.split(qkv, 3, axis=-1)
        q = q.reshape(b, t, H, HD).transpose(0, 2, 1, 3)
        k = k.reshape(b, t, H, HD).transpose(0, 2, 1, 3)
        v = v.reshape(b, t, H, HD).transpose(0, 2, 1, 3)
        scores = jnp.einsum('bhqd,bhkd->bhqk', q, k) * (1.0 / np.sqrt(HD))
        causal = (jnp.arange(t)[:, None] >= jnp.arange(t)[None, :]).astype(scores.dtype)
        scores = scores * causal - (1.0 - causal) * NEG
        attn = jax.nn.softmax(scores, axis=-1)
        out = jnp.einsum('bhqk,bhkd->bhqd', attn, v)
        out = out.transpose(0, 2, 1, 3).reshape(b, t, d)
        proj = out @ w_proj + b_proj
        x = proj + resid
        mu = jnp.mean(x, axis=-1, keepdims=True)
        var = jnp.var(x, axis=-1, keepdims=True)
        return (x - mu) * jax.lax.rsqrt(var + EPS) * ln_gamma + ln_beta

    def _L0_ffn_ref(x, cn_w1, cn_b1, cn_w2, cn_b2, cn_w3, cn_b3, cn_w4, cn_b4, gc_w1, gc_b1, gc_w2, gc_b2, gc_w3, gc_b3, adaptive_range):
        import jax, jax.numpy as jnp
        import numpy as np
        B, S, DIM = (4, 512, 128)
        BASE_COUPLING = 0.1
        NUM_CYCLES = 3

        def _gelu(x):
            return jax.nn.gelu(x, approximate=False)

        def _coupling_net(h, w1, b1, w2, b2, w3, b3, w4, b4):
            h = _gelu(h @ w1 + b1)
            h = _gelu(h @ w2 + b2)
            h = _gelu(h @ w3 + b3)
            return jax.nn.sigmoid(h @ w4 + b4)

        def _global_net(h, w1, b1, w2, b2, w3, b3):
            h = _gelu(h @ w1 + b1)
            h = _gelu(h @ w2 + b2)
            return jax.nn.sigmoid(h @ w3 + b3)

        def _twist(x):
            o_r, o_i, p_r, p_i = jnp.split(x, 4, axis=-1)
            return jnp.concatenate([p_r, -p_i, -o_r, o_i], axis=-1)
        global_context = x.mean(axis=1, keepdims=True)
        gf = _global_net(global_context, gc_w1, gc_b1, gc_w2, gc_b2, gc_w3, gc_b3)
        out = x
        for _ in range(NUM_CYCLES):
            tf = _coupling_net(out, cn_w1, cn_b1, cn_w2, cn_b2, cn_w3, cn_b3, cn_w4, cn_b4)
            combined = 0.7 * gf + 0.3 * tf
            coupling = BASE_COUPLING + adaptive_range * (combined - 0.5) * 2.0
            out = out + coupling * _twist(out)
        return out

    def _L1_attn_ref(x, w_qkv, b_qkv, a_q, b_q, a_v, b_v, w_proj, b_proj):
        import jax, jax.numpy as jnp
        import numpy as np
        B, N, C = (2, 256, 128)
        H = 16
        HD = C // H
        R = 16
        LORA_SCALE = 32.0 / R
        ATTN_SCALE = HD ** (-0.5)
        Bb, Nn, Cc = x.shape
        qkv = (x @ w_qkv + b_qkv).reshape(Bb, Nn, 3, H, HD).transpose(2, 0, 3, 1, 4)
        q, k, v = (qkv[0], qkv[1], qkv[2])
        q = q + jnp.einsum('bhnr,rd->bhnd', jnp.einsum('bhnd,dr->bhnr', q, a_q), b_q) * LORA_SCALE
        v = v + jnp.einsum('bhnr,rd->bhnd', jnp.einsum('bhnd,dr->bhnr', v, a_v), b_v) * LORA_SCALE
        attn = jax.nn.softmax(jnp.einsum('bhnd,bhmd->bhnm', q, k) * ATTN_SCALE, axis=-1)
        out = jnp.einsum('bhnm,bhmd->bhnd', attn, v)
        out = out.transpose(0, 2, 1, 3).reshape(Bb, Nn, Cc)
        return out @ w_proj + b_proj

    def _L1_ffn_ref(x, router, experts_gate, experts_up, experts_down, shared_gate, shared_up, shared_down):
        import jax, jax.numpy as jnp
        import numpy as np
        TOP_K = 2
        NUM_EXPERTS = 8
        b, s, h = x.shape
        E = router.shape[1]
        shared_act = jax.nn.silu(jnp.einsum('bsh,hd->bsd', x, shared_gate))
        shared_up_out = jnp.einsum('bsh,hd->bsd', x, shared_up)
        shared_out = jnp.einsum('bsd,dh->bsh', shared_act * shared_up_out, shared_down)
        router_probs = jax.nn.softmax(jnp.einsum('bsh,he->bse', x, router), axis=-1)
        topk_probs, topk_idx = jax.lax.top_k(router_probs, TOP_K)
        coef = jnp.sum(jax.nn.one_hot(topk_idx, E, dtype=x.dtype) * topk_probs[..., None], axis=2)
        coef = coef.reshape(b * s, E)
        x_flat = x.reshape(b * s, h)
        gate = jnp.einsum('th,ehd->etd', x_flat, experts_gate)
        up = jnp.einsum('th,ehd->etd', x_flat, experts_up)
        expert_out = jnp.einsum('etd,edh->eth', jax.nn.silu(gate) * up, experts_down)
        routed = jnp.einsum('eth,te->th', expert_out, coef)
        return routed.reshape(b, s, h) + shared_out
    x = L0_attn_target
    x = x + 0.5 * _L0_ffn_ref(_layernorm(x, axis=-1), L0_ffn_cn_w1, L0_ffn_cn_b1, L0_ffn_cn_w2, L0_ffn_cn_b2, L0_ffn_cn_w3, L0_ffn_cn_b3, L0_ffn_cn_w4, L0_ffn_cn_b4, L0_ffn_gc_w1, L0_ffn_gc_b1, L0_ffn_gc_w2, L0_ffn_gc_b2, L0_ffn_gc_w3, L0_ffn_gc_b3, L0_ffn_adaptive_range)
    x = x + _L0_attn_ref(_layernorm(x, axis=-1), L0_attn_w_qkv, L0_attn_w_proj, L0_attn_b_proj, L0_attn_ln_gamma, L0_attn_ln_beta)
    x = x + 0.5 * _L0_ffn_ref(_layernorm(x, axis=-1), L0_ffn_cn_w1, L0_ffn_cn_b1, L0_ffn_cn_w2, L0_ffn_cn_b2, L0_ffn_cn_w3, L0_ffn_cn_b3, L0_ffn_cn_w4, L0_ffn_cn_b4, L0_ffn_gc_w1, L0_ffn_gc_b1, L0_ffn_gc_w2, L0_ffn_gc_b2, L0_ffn_gc_w3, L0_ffn_gc_b3, L0_ffn_adaptive_range)
    x = x + 0.5 * _L1_ffn_ref(_layernorm(x, axis=-1), L1_ffn_router, L1_ffn_experts_gate, L1_ffn_experts_up, L1_ffn_experts_down, L1_ffn_shared_gate, L1_ffn_shared_up, L1_ffn_shared_down)
    x = x + _L1_attn_ref(_layernorm(x, axis=-1), L1_attn_w_qkv, L1_attn_b_qkv, L1_attn_a_q, L1_attn_b_q, L1_attn_a_v, L1_attn_b_v, L1_attn_w_proj, L1_attn_b_proj)
    x = x + 0.5 * _L1_ffn_ref(_layernorm(x, axis=-1), L1_ffn_router, L1_ffn_experts_gate, L1_ffn_experts_up, L1_ffn_experts_down, L1_ffn_shared_gate, L1_ffn_shared_up, L1_ffn_shared_down)
    return x

_drawn_inputs = setup_inputs


def setup_inputs(seed=0):
    import zlib

    import numpy as np

    out = dict(_drawn_inputs(seed))
    spreads = {'L0_attn_b_proj': (0.0, 0.1),
     'L0_attn_ln_gamma': (1.0, 0.2),
     'L0_attn_ln_beta': (0.0, 0.1),
     'L0_ffn_cn_b1': (0.0, 0.8),
     'L0_ffn_cn_b2': (0.0, 0.8),
     'L0_ffn_cn_b3': (0.0, 2.0),
     'L0_ffn_gc_b1': (0.0, 0.8),
     'L0_ffn_gc_b2': (0.0, 2.0)}
    factors = {'L0_attn_w_qkv': 8.0,
     'L0_attn_w_proj': 8.0,
     'L0_ffn_cn_w1': 7.541,
     'L0_ffn_cn_w2': 7.144,
     'L0_ffn_cn_w3': 6.127,
     'L0_ffn_cn_w4': 3.95,
     'L0_ffn_gc_w1': 8.0,
     'L0_ffn_gc_w2': 64.0,
     'L0_ffn_gc_w3': 8.0,
     'L1_attn_b_qkv': 7.629,
     'L1_attn_a_q': 8.0,
     'L1_attn_b_q': 8.0,
     'L1_attn_a_v': 8.0,
     'L1_attn_b_v': 8.0,
     'L1_attn_b_proj': 22.322}
    for name, (base, spread) in spreads.items():
        noise = np.random.default_rng([zlib.crc32(name.encode()), seed]).standard_normal(out[name].shape)
        drawn = base * np.exp(spread * noise) if base else spread * noise
        out[name] = jnp.asarray(drawn.astype(out[name].dtype))
    for name, factor in factors.items():
        out[name] = (out[name] * factor).astype(out[name].dtype)
    return out
```

```python
import numpy as np

import concourse.bass as bass
from concourse import mybir
from contextlib import ExitStack

fp32 = mybir.dt.float32
bf16 = mybir.dt.bfloat16
ALU = mybir.AluOpType
ACT = mybir.ActivationFunctionType
AX = mybir.AxisListType

P = 128
N = 2048
CW = 512
NC = N // CW
TW = 128
NT = N // TW
TPC = CW // TW
EPS = 1e-5

CYCLES = 3
H2, H3 = 64, 32
BASE_COUPLING = 0.1

HEADS = 16
HD = P // HEADS
PAIRS = HEADS // 2
SCALE = float(HD) ** -0.5
MASK = -1.0e10 / SCALE
LORA_R = 16
LORA_SCALE = 32.0 / LORA_R
HALF = 64
MAXROW = 32
Q_ROWS = {0: (0, 8, 16), 1: (24, 40), 2: (48,)}
K_ROWS = {0: (0, 24, 48), 1: (8, 40), 2: (16,)}
SUB = P // HEADS
VC = 32
NP = 8
LEAD = 4

EXPERTS = 8
ED = 64
GROUPS = EXPERTS // 2 + 1


def chunk(t, c):
    return t[:, c * CW:(c + 1) * CW]


def tile(t, i):
    return t[:, i * TW:(i + 1) * TW]


class SemBanks:
    SIZE = 24

    def __init__(self, nc, stack):
        self.banks = [[stack.enter_context(nc.semaphore(f"bank{b}_{i}")) for i in range(self.SIZE)] for b in range(2)]
        self.now = 0

    def next_phase(self):
        self.now = 1 - self.now
        return iter(self.banks[self.now])

    def clear_last(self, sp):
        last = self.banks[1 - self.now]
        assert last[-1].num - last[0].num == self.SIZE - 1
        sp.sem_clear(range(last[0].num, last[-1].num + 1))


class Names:

    def __init__(self, nc, stack, prefix, banks=None):
        self.nc, self.stack, self.prefix = nc, stack, prefix
        self.sems = banks.next_phase() if banks else None

    def sem(self, name):
        if self.sems:
            return next(self.sems)
        return self.stack.enter_context(self.nc.semaphore(f"{self.prefix}_{name}"))

    def sb(self, name, shape, dt):
        return self.stack.enter_context(self.nc.sbuf_tensor(f"{self.prefix}_{name}", shape, dt))

    def dram(self, name, shape, dt):
        return self.nc.dram_tensor(f"{self.prefix}_{name}", shape, dt, kind="Internal").ap()


def load_constants(nc, stack, ps, dram, k):
    n = Names(nc, stack, "k")
    for name in ("cn_w1", "cn_w2", "cn_w3", "cn_w4", "gc_w1", "gc_w2", "gc_w3", "router", "s_gate", "s_up", "s_down",
                 "wqkv0", "wproj0", "wqkv1", "wproj1", "wqT1", "wvT1"):
        k[name] = n.sb(name, list(dram[name].shape), fp32)
    for name in ("cn_b1", "cn_b2", "cn_b3", "cn_b4", "gc_b1", "gc_b2", "gc_b3", "arange", "bproj0", "gamma", "beta",
                 "bq1", "bk1", "bv1", "bproj1"):
        k[name] = n.sb(name, list(dram[name].shape), fp32)
    for name in ("aqT", "bq", "avT", "bv"):
        k[name] = n.sb(name, [P, 2, P], fp32)
    k["e_gate"] = n.sb("e_gate", [P, EXPERTS, ED], fp32)
    k["e_up"] = n.sb("e_up", [P, EXPERTS, ED], fp32)
    k["e_down"] = n.sb("e_down", [P, EXPERTS // 2, P], fp32)
    k["mean_of"] = n.sb("mean_of", [P, P], fp32)
    k["first_row"] = n.sb("first_row", [P, P], fp32)
    k["ident"] = n.sb("ident", [P, P], fp32)
    k["identb"] = n.sb("identb", [P, P], bf16)
    k["ones"] = n.sb("ones", [1, P], fp32)
    k["mask_q"] = n.sb("mask_q", [P, TW], bf16)
    k["mask_k"] = n.sb("mask_k", [P, 2 * TW], bf16)
    k["pick"] = n.sb("pick", [3 * EXPERTS, EXPERTS // 2, 2, ED], bf16)
    k["spread"] = n.sb("spread", [P, SUB, HEADS, HD], fp32)
    k["q_op"] = [n.sb(f"q_op{a}", [P, N], bf16) for a in range(2)]
    k["k_op"] = [[n.sb(f"k_op{a}{j}", [P, N], bf16) for j in range(2)] for a in range(2)]
    k["v_op"] = [n.sb(f"v_op{a}", [P, NT, 2, VC], fp32) for a in range(2)]
    k["maxparts"] = n.sb("maxparts", [P, TPC, P], bf16)
    loaded, made, zeroed, v_zeroed = n.sem("loaded"), n.sem("made"), n.sem("zeroed"), n.sem("v_zeroed")
    k["eps"] = n.sb("eps", [P, 1], fp32)
    k["twist"] = n.sb("twist", [P, P], fp32)
    k_names = [name for name in k if name != "x" and name in dram and len(dram[name].shape) == 2]
    loads = [(k[name][:, :], dram[name]) for name in k_names]
    loads += [(k[name][:, :, :], dram[name]) for name in ("aqT", "bq", "avT", "bv")]
    loads += [(k["e_gate"][:, :, :], dram["e_gate"].rearrange("e h d -> h e d")),
              (k["e_up"][:, :, :], dram["e_up"].rearrange("e h d -> h e d")),
              (k["e_down"][:, :, :], dram["e_down"].rearrange("(g e) d h -> (e d) g h", e=2))]
    is_early = [name[:3] in ("cn_", "gc_", "ara") for name in k_names] + [False] * (len(loads) - len(k_names))
    early = [load for load, e in zip(loads, is_early) if e]
    k["late_loads"] = [load for load, e in zip(loads, is_early) if not e]
    with nc.Block() as block:
        @block.sync
        def _(sp):
            sp.dma_start(k["x"][:, :], dram["x"]).then_inc(loaded, 16)
            for dst, src in early:
                sp.dma_start(dst, src).then_inc(loaded, 16)
            sp.wait_ge(loaded, 16 * (len(early) + 1))

        @block.vector
        def _(dve):
            nc.vector.memset(k["mean_of"][:, :], 1.0 / P)
            nc.vector.memset(k["ones"][:, :], 1.0)
            nc.vector.memset(k["eps"][:, :], EPS)
            nc.vector.memset(k["first_row"][:, :], 0.0).then_inc(zeroed, 1)
            dve.wait_ge(zeroed, 1)
            for r in range(0, P, 32):
                nc.vector.memset(k["first_row"][r:r + 1, :], 1.0)
            for a in range(2):
                nc.vector.memset(k["q_op"][a][:, :], 0.0)
                for j in range(2):
                    nc.vector.memset(k["k_op"][a][j][:, :], 0.0).then_inc(zeroed, 1)
            dve.wait_ge(zeroed, 1 + 4)
            for a in range(2):
                for j in range(2):
                    row = HALF * j + MAXROW
                    nc.vector.memset(k["k_op"][a][j][row:row + 3, :], 1.0)

        @block.gpsimd
        def _(pool):
            pool.memset(k["ident"][:, :], 0.0)
            pool.memset(k["identb"][:, :], 0.0)
            pool.memset(k["twist"][:, :], 0.0)
            pool.memset(k["mask_q"][:, :], 0.0)
            pool.memset(k["mask_k"][:, :], MASK)
            pool.memset(k["maxparts"][:, :, :], 0.0)
            for a in range(2):
                pool.memset(k["v_op"][a][:, :, :, :], 0.0).then_inc(v_zeroed, 1)
            pool.memset(k["spread"][:, :, :, :], 1.0)
            pool.memset(k["pick"][:, :, :, :], 1.0).then_inc(made, 1)
            pool.wait_ge(v_zeroed, 2)
            for a in range(2):
                pool.memset(k["v_op"][a][:, :, :, HD:HD + 1], 1.0)
            pool.wait_ge(made, 1)
            pool.affine_select(out=k["spread"][:, :, :, :], in_=k["spread"][:, :, :, :], compare_op=ALU.is_equal,
                               fill=0.0, base=0, pattern=[[-1, SUB], [-SUB, HEADS], [0, HD]], channel_multiplier=1)
            pool.affine_select(out=k["ident"][:, :], in_=k["ident"][:, :], compare_op=ALU.not_equal, fill=1.0,
                               base=0, pattern=[[-1, P]], channel_multiplier=1)
            pool.affine_select(out=k["identb"][:, :], in_=k["identb"][:, :], compare_op=ALU.not_equal, fill=1.0,
                               base=0, pattern=[[-1, P]], channel_multiplier=1)
            for b, (source, sign) in enumerate(((64, 1.0), (96, -1.0), (0, -1.0), (32, 1.0))):
                block_b = k["twist"][:, 32 * b:32 * b + 32]
                pool.affine_select(out=block_b, in_=block_b, compare_op=ALU.not_equal, fill=sign,
                                   base=-source, pattern=[[-1, 32]], channel_multiplier=1)
            pool.affine_select(out=k["mask_q"][:, :], in_=k["mask_q"][:, :], compare_op=ALU.is_ge, fill=MASK,
                               base=0, pattern=[[-1, TW]], channel_multiplier=1)
            pool.affine_select(out=k["mask_k"][:, TW:], in_=k["mask_k"][:, TW:], compare_op=ALU.is_gt, fill=0.0,
                               base=0, pattern=[[-1, TW]], channel_multiplier=1)
            pool.affine_select(out=k["pick"][:, :, :, :], in_=k["pick"][:, :, :, :], compare_op=ALU.is_equal,
                               fill=0.0, base=0, pattern=[[-2, EXPERTS // 2], [-1, 2], [0, ED]],
                               channel_multiplier=1).then_inc(made, 1)
            pool.wait_ge(made, 2)
            for part in (1, 2):
                pool.affine_select(out=k["pick"][:, :, :, :], in_=k["pick"][:, :, :, :], compare_op=ALU.not_equal,
                                   fill=1.0, base=-EXPERTS * part,
                                   pattern=[[-2, EXPERTS // 2], [-1, 2], [0, ED]],
                                   channel_multiplier=1).then_inc(made, 1)
                pool.wait_ge(made, 2 + part)


def layernorm(nc, prefix, ps, k, src, dst, gamma=None, beta=None, add_to=None):
    with ExitStack() as stack:
        n = Names(nc, stack, prefix, k["banks"])
        cen, sq, std, rstd = (k[name] for name in ("cen", "sq", "std", "rstd"))
        mean_ready, centred, squared = n.sem("mean_ready"), n.sem("centred"), n.sem("squared")
        var_ready, std_ready, rstd_ready = n.sem("var_ready"), n.sem("std_ready"), n.sem("rstd_ready")
        spread, normed = n.sem("spread"), n.sem("normed")
        with nc.Block() as block:
            @block.sync
            def _(sp):
                k["banks"].clear_last(sp)

            @block.tensor
            def _(pe):
                for c in range(NC):
                    pe.matmul(ps[:, c, :], k["mean_of"][:, :], chunk(src, c), start=True, stop=True)\
                        .then_inc(mean_ready, 1)
                for c in range(NC):
                    pe.wait_ge(squared, c + 1)
                    pe.matmul(ps[32 * c:32 * c + 32, NC, :], k["mean_of"][:, 0:32], chunk(sq, c),
                              start=True, stop=True).then_inc(var_ready, 1)
                pe.wait_ge(rstd_ready, 1)
                for c in range(NC):
                    pe.matmul(ps[:, c, :], k["first_row"][32 * c:32 * c + 32, :], rstd[32 * c:32 * c + 32, :],
                              start=True, stop=True).then_inc(spread, 1)

            @block.vector
            def _(dve):
                for c in range(NC):
                    dve.wait_ge(mean_ready, c + 1)
                    nc.vector.tensor_tensor(chunk(cen, c), chunk(src, c), ps[:, c, :], ALU.subtract)\
                        .then_inc(centred, 1)
                dve.wait_ge(std_ready, 1)
                nc.vector.reciprocal(rstd[:, :], std[:, :]).then_inc(rstd_ready, 1)
                for c in range(NC):
                    dve.wait_ge(spread, c + 1)
                    if add_to is None:
                        nc.vector.tensor_tensor(chunk(dst, c), chunk(cen, c), ps[:, c, :], ALU.mult)
                        continue
                    nc.vector.scalar_tensor_tensor(out=chunk(cen, c), in0=chunk(cen, c), scalar=gamma,
                                                   in1=ps[:, c, :], op0=ALU.mult, op1=ALU.mult)\
                        .then_inc(normed, 1)
                    dve.wait_ge(normed, c + 1)
                    nc.vector.scalar_tensor_tensor(out=chunk(add_to, c), in0=chunk(cen, c), scalar=beta,
                                                   in1=chunk(add_to, c), op0=ALU.add, op1=ALU.add)

            @block.scalar
            def _(act):
                for c in range(NC):
                    act.wait_ge(centred, c + 1)
                    nc.scalar.activation(chunk(sq, c), chunk(cen, c), ACT.Square).then_inc(squared, 1)
                act.wait_ge(var_ready, NC)
                nc.scalar.activation(std[:, :], ps[:, NC, :], ACT.Sqrt, bias=k["eps"][:, 0:1]).then_inc(std_ready, 1)


def coupled_ffn(nc, prefix, ps, k, xn, x):
    with ExitStack() as stack:
        n = Names(nc, stack, prefix, k["banks"])
        total = n.sb("total", [P, 1], fp32)
        g1, g2, gt = n.sb("g1", [H2, 1], fp32), n.sb("g2", [H3, 1], fp32), n.sb("gt", [P, 1], fp32)
        u, c0, c1 = n.sb("u", [P, 3], fp32), n.sb("c0", [P, 1], fp32), n.sb("c1", [P, 1], fp32)
        hb4, ghb3 = n.sb("hb4", [P, 1], fp32), n.sb("ghb3", [P, 1], fp32)
        h1, h2, h3 = n.sb("h1", [P, N], fp32), n.sb("h2", [P, 2, CW], fp32), n.sb("h3", [P, CW], fp32)
        th, cp, tw = n.sb("th", [P, N], fp32), n.sb("cp", [P, N], fp32), n.sb("tw", [P, N], fp32)
        summed, halves, weights_in = n.sem("summed"), n.sem("halves"), n.sem("weights_in")
        g_mm, g_act, scal = n.sem("g_mm"), n.sem("g_act"), n.sem("scal")
        w1_done, h1_ready, w2_done, h2_ready = n.sem("w1_done"), n.sem("h1_ready"), n.sem("w2_done"), n.sem("h2_ready")
        w3_done, h3_ready, w4_done, th_ready = n.sem("w3_done"), n.sem("h3_ready"), n.sem("w4_done"), n.sem("th_ready")
        tw_done, cp_ready, tw_ready, updated = n.sem("tw_done"), n.sem("cp_ready"), n.sem("tw_ready"), n.sem("updated")
        with nc.Block() as block:
            @block.sync
            def _(sp):
                k["banks"].clear_last(sp)
                for dst, src in k["late_loads"]:
                    sp.dma_start(dst, src).then_inc(weights_in, 16)
                if k["late_loads"]:
                    sp.wait_ge(weights_in, 16 * len(k["late_loads"]))
                k["late_loads"] = []

            @block.tensor
            def _(pe):
                for s in range(CYCLES):
                    for c in range(NC):
                        if s > 0:
                            pe.wait_ge(updated, NC * (s - 1) + c + 1)
                        pe.matmul(ps[:, c, :], k["cn_w1"][:, :], chunk(xn, c), start=True, stop=True)\
                            .then_inc(w1_done, 1)
                    for c in range(NC):
                        pe.wait_ge(h1_ready, NC * s + c + 1)
                        if s > 0:
                            pe.wait_ge(tw_ready, NC * s)
                        lo = H2 * (c % 2)
                        pe.matmul(ps[lo:lo + H2, NC + c // 2, :], k["cn_w2"][:, :], chunk(h1, c),
                                  start=True, stop=True).then_inc(w2_done, 1)
                    for c in range(NC):
                        pe.wait_ge(h2_ready, 2 * s + c // 2 + 1)
                        lo = H2 * (c % 2)
                        pe.matmul(ps[H3 * c:H3 * c + H3, NC + 2, :], k["cn_w3"][lo:lo + H2, :],
                                  h2[lo:lo + H2, c // 2, :], start=True, stop=True).then_inc(w3_done, 1)
                    if s == 0:
                        pe.wait_ge(summed, 1)
                        pe.matmul(ps[0:H2, 7, 0:1], k["gc_w1"][:, :], total[:, :], start=True, stop=True)\
                            .then_inc(g_mm, 1)
                        pe.wait_ge(g_act, 1)
                        pe.matmul(ps[0:H3, 7, 1:2], k["gc_w2"][:, :], g1[:, :], start=True, stop=True)\
                            .then_inc(g_mm, 1)
                        pe.wait_ge(g_act, 2)
                        pe.matmul(ps[:, 7, 2:3], k["gc_w3"][:, :], g2[:, :], start=True, stop=True)\
                            .then_inc(g_mm, 1)
                    pe.wait_ge(h3_ready, s + 1)
                    for c in range(NC):
                        pe.matmul(ps[:, c, :], k["cn_w4"][H3 * c:H3 * c + H3, :], h3[H3 * c:H3 * c + H3, :],
                                  start=True, stop=True).then_inc(w4_done, 1)
                        if s == 0 and c == NC - 1:
                            pe.wait_ge(g_act, 3)
                        pe.matmul(ps[:, NC + c, :], k["twist"][:, :], chunk(xn, c), start=True, stop=True)\
                            .then_inc(tw_done, 1)

            @block.scalar
            def _(act):
                nc.scalar.activation(hb4[:, :], k["cn_b4"][:, :], ACT.Copy, scale=0.5).then_inc(halves, 1)
                nc.scalar.activation(ghb3[:, :], k["gc_b3"][:, :], ACT.Copy, scale=0.5).then_inc(halves, 1)
                act.wait_ge(halves, 2)
                for s in range(CYCLES):
                    for c in range(NC):
                        act.wait_ge(w1_done, NC * s + c + 1)
                        nc.scalar.activation(chunk(h1, c), ps[:, c, :], ACT.Gelu, bias=k["cn_b1"][:, 0:1])\
                            .then_inc(h1_ready, 1)
                    for g in range(2):
                        act.wait_ge(w2_done, NC * s + 2 * g + 2)
                        nc.scalar.activation(h2[:, g, :], ps[:, NC + g, :], ACT.Gelu, bias=k["cn_b2"][:, 0:1])\
                            .then_inc(h2_ready, 1)
                    act.wait_ge(w3_done, NC * (s + 1))
                    nc.scalar.activation(h3[:, :], ps[:, NC + 2, :], ACT.Gelu, bias=k["cn_b3"][:, 0:1])\
                        .then_inc(h3_ready, 1)
                    if s == 0:
                        act.wait_ge(g_mm, 1)
                        nc.scalar.activation(g1[:, :], ps[0:H2, 7, 0:1], ACT.Gelu, bias=k["gc_b1"][:, 0:1],
                                             scale=1.0 / N).then_inc(g_act, 1)
                        act.wait_ge(g_mm, 2)
                        nc.scalar.activation(g2[:, :], ps[0:H3, 7, 1:2], ACT.Gelu, bias=k["gc_b2"][:, 0:1])\
                            .then_inc(g_act, 1)
                        act.wait_ge(g_mm, 3)
                        nc.scalar.activation(gt[:, :], ps[:, 7, 2:3], ACT.Tanh, bias=ghb3[:, 0:1], scale=0.5)\
                            .then_inc(g_act, 1)
                    for c in range(NC):
                        act.wait_ge(w4_done, NC * s + c + 1)
                        if s > 0:
                            act.wait_ge(cp_ready, NC * (s - 1) + c + 1)
                        nc.scalar.activation(chunk(th, c), ps[:, c, :], ACT.Tanh, bias=hb4[:, 0:1], scale=0.5)\
                            .then_inc(th_ready, 1)

            @block.vector
            def _(dve):
                nc.vector.tensor_reduce(total[:, :], xn[:, :], AX.X, ALU.add).then_inc(summed, 1)
                dve.wait_ge(g_act, 3)
                nc.vector.tensor_scalar(u[:, 0:1], gt[:, :], 0.5, 0.5, ALU.mult, ALU.add).then_inc(scal, 1)
                dve.wait_ge(scal, 1)
                nc.vector.tensor_scalar(u[:, 1:2], u[:, 0:1], 0.7, 0.15 - 0.5, ALU.mult, ALU.add).then_inc(scal, 1)
                nc.vector.tensor_scalar(u[:, 2:3], k["arange"][:, :], 2.0, None, ALU.mult).then_inc(scal, 1)
                dve.wait_ge(scal, 3)
                nc.vector.tensor_scalar(c0[:, :], u[:, 1:2], u[:, 2:3], BASE_COUPLING, ALU.mult, ALU.add)\
                    .then_inc(scal, 1)
                nc.vector.tensor_scalar(c1[:, :], u[:, 2:3], 0.15, None, ALU.mult).then_inc(scal, 1)
                dve.wait_ge(scal, 5)
                for s in range(CYCLES):
                    for c in range(NC):
                        i = NC * s + c + 1
                        dve.wait_ge(th_ready, i)
                        nc.vector.tensor_scalar(chunk(cp, c), chunk(th, c), c1[:, 0:1], c0[:, 0:1], ALU.mult, ALU.add)\
                            .then_inc(cp_ready, 1)
                        dve.wait_ge(tw_done, i)
                        dve.wait_ge(cp_ready, i)
                        nc.vector.tensor_tensor(chunk(tw, c), chunk(cp, c), ps[:, NC + c, :], ALU.mult)\
                            .then_inc(tw_ready, 1)
                        dve.wait_ge(tw_ready, i)
                        nc.vector.tensor_tensor(chunk(xn, c), chunk(xn, c), chunk(tw, c), ALU.add)\
                            .then_inc(updated, 1)
                        if s == CYCLES - 1:
                            dve.wait_ge(updated, i)
                            nc.vector.scalar_tensor_tensor(out=chunk(x, c), in0=chunk(xn, c), scalar=0.5,
                                                           in1=chunk(x, c), op0=ALU.mult, op1=ALU.add)


def moe_ffn(nc, prefix, ps, k, xn, x):
    with ExitStack() as stack:
        n = Names(nc, stack, prefix, k["banks"])
        E = EXPERTS
        rows = [P, NT, E]
        lg, pr, pa, sc = n.sb("lg", rows, fp32), n.sb("pr", rows, fp32), n.sb("pa", rows, fp32), n.sb("sc", rows, fp32)
        rank, coef = n.sb("rank", rows, fp32), n.sb("coef", rows, fp32)
        one = [n.sb(f"one{r}", rows, fp32) for r in range(2)]
        top, rsum = n.sb("top", [P, NT, 1], fp32), n.sb("rsum", [P, NT, 1], fp32)
        parts = n.sb("parts", [P, NT, 3, E], bf16)
        coefT = n.sb("coefT", [3 * E, N], bf16)
        act_g = n.sb("act_g", [P, 2, CW], fp32)
        hid_a = n.sb("hid_a", [P, 2, CW], fp32)
        hid = n.sb("hid", [P, 2, CW], fp32)
        routed, chain, exped, parted = n.sem("routed"), n.sem("chain"), n.sem("exped"), n.sem("parted")
        turned, coef_ready, lg_ready = n.sem("turned"), n.sem("coef_ready"), n.sem("lg_ready")
        gate_done, up_done, silued, gated = n.sem("gate_done"), n.sem("up_done"), n.sem("silued"), n.sem("gated")
        bc_done, hid_ready, down_done, added = n.sem("bc_done"), n.sem("hid_ready"), n.sem("down_done"), n.sem("added")
        steps = [(c, g) for c in range(NC) for g in range(GROUPS)]

        def bcs(i):
            return i - i // GROUPS

        turn = ps[:, 6, :].bitcast(bf16)

        with nc.Block() as block:
            @block.sync
            def _(sp):
                k["banks"].clear_last(sp)

            @block.tensor
            def _(pe):
                for t in range(NT):
                    mm = pe.matmul(ps[:, 7, E * t:E * t + E], tile(xn, t), k["router"][:, :], start=True, stop=True)
                mm.then_inc(routed, 1)

                def gate_up(i):
                    c, g = steps[i]
                    if i >= 2:
                        pe.wait_ge(silued, i - 1)
                        pe.wait_ge(hid_ready, i - 1)
                    shared = g == GROUPS - 1
                    wg = k["s_gate"][:, :] if shared else k["e_gate"][:, 2 * g:2 * g + 2, :].rearrange("p e d -> p (e d)")
                    wu = k["s_up"][:, :] if shared else k["e_up"][:, 2 * g:2 * g + 2, :].rearrange("p e d -> p (e d)")
                    pe.matmul(ps[:, i % 2, :], wg, chunk(xn, c), start=True, stop=True).then_inc(gate_done, 1)
                    pe.matmul(ps[:, 2 + i % 2, :], wu, chunk(xn, c), start=True, stop=True).then_inc(up_done, 1)

                def down(i):
                    c, g = steps[i]
                    if g == 0 and c >= 2:
                        pe.wait_ge(added, c - 1)
                    if g == 0 and c == 0:
                        pe.wait_ge(coef_ready, NC)
                    pe.wait_ge(hid_ready, i + 1)
                    wd = k["s_down"][:, :] if g == GROUPS - 1 else k["e_down"][:, g, :]
                    mm = pe.matmul(ps[:, 6 + c % 2, :], wd, hid[:, i % 2, :], start=(g == 0), stop=(g == GROUPS - 1))
                    mm.then_inc(down_done, 1)

                gate_up(0)
                gate_up(1)
                for c in range(NC):
                    if c == 0:
                        pe.wait_ge(parted, 3)
                    else:
                        pe.wait_ge(coef_ready, c)
                    for t in range(TPC * c, TPC * c + TPC):
                        o = TW * (t % TPC)
                        mm = pe.transpose(turn[0:3 * E, o:o + TW], parts[:, t, :, :].rearrange("p a e -> p (a e)"),
                                          k["identb"][:, :])
                    mm.then_inc(turned, 1)
                pe.wait_ge(coef_ready, NC)

                def coefficients(i):
                    c, g = steps[i]
                    if g == GROUPS - 1:
                        return
                    b = bcs(i)
                    if b >= 2:
                        pe.wait_ge(hid_ready, i - 1)
                    pe.matmul(ps[:, 4 + b % 2, :], k["pick"][:, g, :, :].rearrange("p a e -> p (a e)"),
                              chunk(coefT, c), start=True, stop=True).then_inc(bc_done, 1)

                coefficients(0)
                for i in range(len(steps)):
                    if i + 1 < len(steps):
                        coefficients(i + 1)
                    if i >= 1:
                        down(i - 1)
                    if i + 2 < len(steps):
                        gate_up(i + 2)
                down(len(steps) - 1)

            @block.scalar
            def _(act):
                act.wait_ge(lg_ready, 1)
                nc.scalar.activation(pr[:, :, :], lg[:, :, :], ACT.Exp).then_inc(exped, 1)
                for c in range(NC):
                    act.wait_ge(turned, c + 1)
                    nc.scalar.activation(chunk(coefT, c), turn[0:3 * E, 0:CW], ACT.Copy).then_inc(coef_ready, 1)
                for i in range(len(steps)):
                    act.wait_ge(gate_done, i + 1)
                    if i >= 2:
                        act.wait_ge(hid_ready, i - 1)
                    nc.scalar.activation(act_g[:, i % 2, :], ps[:, i % 2, :], ACT.Silu).then_inc(silued, 1)

            @block.vector
            def _(dve):
                links = [0]

                def link(ins):
                    links[0] += 1
                    ins.then_inc(chain, 1)
                    dve.wait_ge(chain, links[0])

                scores = ps[:, 7, 0:NT * E].rearrange("p (t e) -> p t e", e=E)
                spread = lambda a: a[:, :, :].to_broadcast(rows)
                dve.wait_ge(routed, 1)
                link(nc.vector.tensor_reduce(top[:, :, 0], scores, AX.X, ALU.max))
                nc.vector.tensor_tensor(lg[:, :, :], scores, spread(top), ALU.subtract).then_inc(lg_ready, 1)
                for e in range(E):
                    nc.vector.memset(rank[:, :, e], float(E - e))
                dve.wait_ge(exped, 1)
                link(nc.vector.tensor_reduce(rsum[:, :, 0], pr[:, :, :], AX.X, ALU.add))
                link(nc.vector.reciprocal(rsum[:, :, :], rsum[:, :, :]))
                link(nc.vector.tensor_tensor(pr[:, :, :], pr[:, :, :], spread(rsum), ALU.mult))
                left = pr
                for r in range(2):
                    link(nc.vector.tensor_reduce(top[:, :, 0], left[:, :, :], AX.X, ALU.max))
                    link(nc.vector.tensor_tensor(sc[:, :, :], left[:, :, :], spread(top), ALU.is_equal))
                    link(nc.vector.tensor_tensor(sc[:, :, :], sc[:, :, :], rank[:, :, :], ALU.mult))
                    link(nc.vector.tensor_reduce(top[:, :, 0], sc[:, :, :], AX.X, ALU.max))
                    link(nc.vector.tensor_tensor(one[r][:, :, :], sc[:, :, :], spread(top), ALU.is_equal))
                    if r == 0:
                        link(nc.vector.scalar_tensor_tensor(out=pa[:, :, :], in0=one[0][:, :, :], scalar=-2.0,
                                                            in1=pr[:, :, :], op0=ALU.mult, op1=ALU.add))
                        left = pa
                link(nc.vector.tensor_tensor(sc[:, :, :], one[0][:, :, :], one[1][:, :, :], ALU.add))
                link(nc.vector.tensor_tensor(coef[:, :, :], sc[:, :, :], pr[:, :, :], ALU.mult))
                nc.vector.tensor_copy(parts[:, :, 0, :], coef[:, :, :]).then_inc(parted, 1)
                dve.wait_ge(parted, 1)
                link(nc.vector.tensor_tensor(sc[:, :, :], coef[:, :, :], parts[:, :, 0, :], ALU.subtract))
                nc.vector.tensor_copy(parts[:, :, 1, :], sc[:, :, :]).then_inc(parted, 1)
                dve.wait_ge(parted, 2)
                nc.vector.tensor_tensor(parts[:, :, 2, :], sc[:, :, :], parts[:, :, 1, :], ALU.subtract)\
                    .then_inc(parted, 1)
                for i, (c, g) in enumerate(steps):
                    dve.wait_ge(up_done, i + 1)
                    dve.wait_ge(silued, i + 1)
                    if i >= 2:
                        dve.wait_ge(down_done, i - 1)
                    if g == GROUPS - 1:
                        nc.vector.tensor_tensor(hid[:, i % 2, :], act_g[:, i % 2, :], ps[:, 2 + i % 2, :], ALU.mult)\
                            .then_inc(hid_ready, 1)
                    else:
                        nc.vector.tensor_tensor(hid_a[:, i % 2, :], act_g[:, i % 2, :], ps[:, 2 + i % 2, :], ALU.mult)\
                            .then_inc(gated, 1)
                        dve.wait_ge(bc_done, bcs(i) + 1)
                        dve.wait_ge(gated, bcs(i) + 1)
                        nc.vector.tensor_tensor(hid[:, i % 2, :], hid_a[:, i % 2, :], ps[:, 4 + bcs(i) % 2, :], ALU.mult)\
                            .then_inc(hid_ready, 1)
                    if g == 0 and c >= 1:
                        dve.wait_ge(down_done, i)
                        nc.vector.scalar_tensor_tensor(out=chunk(x, c - 1), in0=ps[:, 6 + (c - 1) % 2, :], scalar=0.5,
                                                       in1=chunk(x, c - 1), op0=ALU.mult, op1=ALU.add)\
                            .then_inc(added, 1)
                dve.wait_ge(down_done, len(steps))
                c = NC - 1
                nc.vector.scalar_tensor_tensor(out=chunk(x, c), in0=ps[:, 6 + c % 2, :], scalar=0.5,
                                               in1=chunk(x, c), op0=ALU.mult, op1=ALU.add)


TURN_SEMS = ["q_in0", "q_in1", "k_in0", "k_in1", "v_ready", "mx_filled", "mx_used", "max_ready", "max_split",
             "q_ready", "st_filled", "prob_ready", "pv_done", "sums_ready", "sums_sent0", "sums_sent1"]


class Plan:
    RING = 2 * NC

    def __init__(self, causal):
        self.causal = causal
        self.turn, self.before = [], []
        for n in range(self.RING):
            self.turn += self.window(n)
        self.before = [("fill", 0, f) for f in range(len(self.fills(0)))]
        self.before += [("fill", 1, f) for f in range(LEAD)] + [("max", 0, 0)]

    def keys(self, n):
        return TPC * (n % NC) + TPC if self.causal else NT

    def fills(self, n):
        if not self.causal:
            return [(q, j, CW) for q in range(TPC) for j in range(NC)]
        c = n % NC
        return [(q, j, CW if j < c else TW * (q + 1)) for q in range(TPC) for j in range(c + 1)]

    def first_query(self, n, kt):
        r = kt - TPC * (n % NC)
        if not self.causal or r < 0:
            return 0, None
        if n % NC == 0 and kt == 1:
            return 0, k_slice(0, 2 * TW)
        return TW * r, k_slice(TW, 2 * TW)

    def window(self, n):
        last = len(self.fills(n + 1))
        fills = [("fill", n + 1, f) for f in range(LEAD, last)] + [("fill", n + 2, f) for f in range(LEAD)]
        own, steps, out, done, maxed = last - LEAD, self.keys(n), [], 0, False
        for i in range(steps):
            out.append(("exp", n, i))
            upto = (i + 1) * len(fills) // steps
            out += fills[done:upto]
            done = upto
            if not maxed and (done >= own + 3 or i == steps - 1):
                out.append(("max", n + 1, 0))
                maxed = True
        return out


def k_slice(a, b):
    return slice(a, b)


def attention(nc, prefix, ps, k, xn, x, wqkv, wproj, bproj, causal, lora):
    plan = Plan(causal)
    with ExitStack() as outer:
        n = Names(nc, outer, prefix)
        parts_dram = n.dram("parts", [2, 3, P + 2 * HD, N], bf16)
        sums_dram = n.dram("sums", [2, P, N], fp32), n.dram("psums", [2, HEADS, N], fp32)
        v_all = n.sb("v_all", [P, NT, P + 2 * HD], fp32)
        project_qkv(nc, prefix + "p", ps, k, xn, wqkv, lora, parts_dram, v_all)
        attend(nc, prefix + "l", ps, k, plan, parts_dram, v_all, sums_dram)
        project_out(nc, prefix + "o", ps, k, xn, x, wproj, bproj, causal, sums_dram)


def project_qkv(nc, prefix, ps, k, xn, wqkv, lora, parts_dram, v_all):
    with ExitStack() as stack:
        n = Names(nc, stack, prefix, k["banks"])
        bd = {name: n.sb("bd" + name, [P, P], fp32) for name in "qv"}
        wl = {name: n.sb("w" + name, [P, P], fp32) for name in "qv"}
        bias = {"q": n.sb("biasq", [P, 1], fp32), "k": k["bk1"]}
        bias_v = n.sb("bias_v", [1, P], fp32)
        full = n.sb("full", [P, 2, CW], fp32)
        rest = n.sb("rest", [P, 2, CW], fp32)
        part = n.sb("part", [P, 2, 3, N], bf16)
        bd_mm, bd_ready, w_mm, w_ready = n.sem("bd_mm"), n.sem("bd_ready"), n.sem("w_mm"), n.sem("w_ready")
        qk_done, full_ready, split, sent = n.sem("qk_done"), n.sem("full_ready"), n.sem("split"), n.sem("sent")
        v_done, v_copied = n.sem("v_done"), n.sem("v_copied")
        items = [(w, c) for w in range(2) for c in range(NC)]
        lora_parts = (("q", "aqT", "bq", "wqT1"), ("v", "avT", "bv", "wvT1"))
        weights = [wl["q"][:, :] if lora else wqkv[:, 0:P], wqkv[:, P:2 * P]]
        weight_v = wl["v"][:, :] if lora else wqkv[:, 2 * P:3 * P]
        with nc.Block() as block:
            @block.tensor
            def _(pe):
                if lora:
                    for b, (name, a_t, b_m, _) in enumerate(lora_parts):
                        for u in range(2):
                            mm = pe.matmul(ps[:, b, 0:P], k[a_t][:, u, :], k[b_m][:, u, :], start=(u == 0), stop=(u == 1))
                        mm.then_inc(bd_mm, 1)
                    for b, (name, _, _, w_t) in enumerate(lora_parts):
                        pe.wait_ge(bd_ready, b + 1)
                        pe.matmul(ps[:, 2 + b, 0:P], k[w_t][:, :], bd[name][:, :], start=True, stop=True)
                        if name == "q":
                            pe.matmul(ps[:, 4, 0:1], bd[name][:, :], k["bq1"][:, :], start=True, stop=True)\
                                .then_inc(w_mm, 1)
                        else:
                            pe.matmul(ps[0:1, 5, 0:P], k["bv1"][:, :], bd[name][:, :], start=True, stop=True)\
                                .then_inc(w_mm, 1)
                    pe.wait_ge(w_ready, 4)
                for i, (w, c) in enumerate(items):
                    if i >= 4:
                        pe.wait_ge(full_ready, i - 3)
                    pe.matmul(ps[:, i % 4, :], weights[w], chunk(xn, c), start=True, stop=True).then_inc(qk_done, 1)
                for t in range(NT):
                    out = ps[:, 4 + t // TPC, TW * (t % TPC):TW * (t % TPC) + TW]
                    mm = pe.matmul(out, tile(xn, t), weight_v, start=True, stop=not lora)
                    if lora:
                        mm = pe.matmul(out, k["ones"][:, :], bias_v[:, :], start=False, stop=True)
                    if t % TPC == TPC - 1:
                        mm.then_inc(v_done, 1)

            @block.scalar
            def _(act):
                for i in range(len(items)):
                    w, c = items[i]
                    act.wait_ge(qk_done, i + 1)
                    if i >= 2:
                        act.wait_ge(split, 4 * (i - 1))
                    if lora:
                        nc.scalar.activation(full[:, i % 2, :], ps[:, i % 4, :], ACT.Identity,
                                             bias=bias["qk"[w]][:, 0:1]).then_inc(full_ready, 1)
                    else:
                        nc.scalar.activation(full[:, i % 2, :], ps[:, i % 4, :], ACT.Copy).then_inc(full_ready, 1)
                for g in range(NT // TPC):
                    act.wait_ge(v_done, g + 1)
                    nc.scalar.activation(v_all[:, TPC * g:TPC * g + TPC, 0:P],
                                         ps[:, 4 + g, :].rearrange("p (t f) -> p t f", f=P), ACT.Copy)

            @block.vector
            def _(dve):
                if lora:
                    for b, (name, _, _, _) in enumerate(lora_parts):
                        dve.wait_ge(bd_mm, b + 1)
                        nc.vector.scalar_tensor_tensor(out=bd[name][:, :], in0=ps[:, b, 0:P], scalar=LORA_SCALE,
                                                       in1=k["ident"][:, :], op0=ALU.mult, op1=ALU.add)\
                            .then_inc(bd_ready, 1)
                    for b, (name, _, _, _) in enumerate(lora_parts):
                        dve.wait_ge(w_mm, b + 1)
                        nc.vector.tensor_copy(wl[name][:, :], ps[:, 2 + b, 0:P]).then_inc(w_ready, 1)
                    nc.vector.tensor_copy(bias["q"][:, :], ps[:, 4, 0:1]).then_inc(w_ready, 1)
                    nc.vector.tensor_copy(bias_v[:, :], ps[0:1, 5, 0:P]).then_inc(w_ready, 1)
                for i, (w, c) in enumerate(items):
                    dve.wait_ge(full_ready, i + 1)
                    f, r = full[:, i % 2, :], rest[:, i % 2, :]
                    hi, mid, lo = (chunk(part[:, w, j, :], c) for j in range(3))
                    nc.vector.tensor_copy(hi, f).then_inc(split, 1)
                    dve.wait_ge(split, 4 * i + 1)
                    nc.vector.tensor_tensor(r, f, hi, ALU.subtract).then_inc(split, 1)
                    dve.wait_ge(split, 4 * i + 2)
                    nc.vector.tensor_copy(mid, r).then_inc(split, 1)
                    dve.wait_ge(split, 4 * i + 3)
                    nc.vector.tensor_tensor(lo, r, mid, ALU.subtract).then_inc(split, 1)

            @block.gpsimd
            def _(pool):
                pool.memset(v_all[:, :, P:], 0.0)

            @block.sync
            def _(sp):
                k["banks"].clear_last(sp)
                for w in range(2):
                    sp.wait_ge(split, 4 * NC * (w + 1))
                    for j in range(3):
                        sp.dma_start(parts_dram[w, j, 0:P, :], part[:, w, j, :]).then_inc(sent, 16)
                        sp.dma_start(parts_dram[w, j, P:, :], part[0:2 * HD, w, j, :]).then_inc(sent, 16)
                sp.wait_ge(sent, 16 * 12)


def attend(nc, prefix, ps, k, plan, parts_dram, v_all, sums_dram):
    RING = plan.RING
    ST, SUM, MX = 3, 3, 4
    with ExitStack() as stack:
        n = Names(nc, stack, prefix, k["banks"])
        q_op, k_op, v_op, maxparts = (k[name] for name in ("q_op", "k_op", "v_op", "maxparts"))
        q_max = [n.sb(f"q_max{a}", [P, CW], bf16) for a in range(2)]
        blockmax = [n.sb(f"blockmax{a}", [P, TPC, 2, NC], fp32) for a in range(2)]
        negmax = n.sb("negmax", [P, TPC, 2], fp32)
        maxrest = n.sb("maxrest", [P, TPC, 2], fp32)
        prob = n.sb("prob", [P, NP, CW], fp32)
        sums = n.sb("sums", [P, 2, CW], fp32)
        s, loop_sems = k["turn_sems"], k["turn_sem_range"]

        def load_pair(sp, a, row):
            for w, (ops, rows, sem) in enumerate((([q_op[a]] * 2, Q_ROWS, s[f"q_in{a}"]), (k_op[a], K_ROWS, s[f"k_in{a}"]))):
                for j, op in enumerate(ops):
                    for p, firsts in rows.items():
                        for r in firsts:
                            sp.dma_start(op[HALF * j + r:HALF * j + r + HD, :],
                                         parts_dram[w, p, bass.ds(row + HD * j, HD), :]).then_inc(sem, 16)

        LOADED = 16 * 2 * 6

        with nc.Block() as block:
            @block.sync
            def _(sp):
                k["banks"].clear_last(sp)
                load_pair(sp, 0, 0)
                sp.wait_ge(s["q_in0"], LOADED)
                sp.wait_ge(s["k_in0"], LOADED)

            @block.gpsimd
            def _(pool):
                pool.tensor_copy(v_op[0][:, :, :, 0:HD], v_all[:, :, 0:2 * HD].rearrange("p t (j d) -> p t j d", d=HD))
        nc.all_engine_barrier(sems_to_clear=loop_sems)

        def run(order, turn):
            uses = [o for o in order if o[0] != "exp"]
            exps = [o for o in order if o[0] == "exp"]
            use_no = {o: i for i, o in enumerate(uses)}
            exp_no = {(m, i): e for e, (_, m, i) in enumerate(exps)}
            maxes = [o for o in uses if o[0] == "max"]
            max_no = {o[1]: i for i, o in enumerate(maxes)}
            fill_count = {}
            batches = [(m, b) for m in range(RING) for b in range(plan.keys(m) // 2)] if exps else []
            batch_no = {mb: i for i, mb in enumerate(batches)}

            def last_batch(m):
                return batch_no[m, plan.keys(m) // 2 - 1]

            with nc.Block() as block:
                @block.tensor
                def _(pe):
                    def fill(m, f):
                        u = use_no["fill", m, f]
                        qt, kc, w = plan.fills(m)[f]
                        a, c = m // NC % 2, m % NC
                        if turn is not None and f == 0 and m in (NC, 2 * NC):
                            pe.wait_ge(s[f"q_in{a}"], LOADED)
                            pe.wait_ge(s[f"k_in{a}"], LOADED)
                        if u >= 2:
                            pe.wait_ge(s["mx_used"], u - 1)
                        masked = plan.causal and kc == c
                        for j in range(2):
                            out = ps[:, MX + 2 * (u % 2) + j, 0:w]
                            q0 = CW * c + TW * qt
                            mm = pe.matmul(out, q_op[a][:, q0:q0 + TW], k_op[a][j][:, CW * kc:CW * kc + w],
                                           start=True, stop=True)
                        if masked:
                            for j in range(2):
                                mm = pe.matmul(ps[:, MX + 2 * (u % 2) + j, w - TW:w], k["identb"][:, :],
                                               k["mask_q"][:, :], start=False, stop=True, skip_group_check=True)
                        mm.then_inc(s["mx_filled"], 1)

                    def turn_max(m):
                        u = use_no["max", m, 0]
                        if u >= 2:
                            pe.wait_ge(s["mx_used"], u - 1)
                        pe.wait_ge(s["max_split"], 4 * max_no[m] + 4)
                        for qt in range(TPC):
                            mm = pe.matmul(ps[:, MX + 2 * (u % 2), TW * qt:TW * qt + TW], maxparts[:, qt, :],
                                           k["identb"][:, :], start=True, stop=True)
                        mm.then_inc(s["mx_filled"], 1)

                    def scores(m, i):
                        a = m // NC % 2
                        if i == 0 and m > 0:
                            pe.wait_ge(s["q_ready"], max_no[m] + 1)
                        q0, mask = plan.first_query(m, i)
                        for j in range(2):
                            e = 2 * exp_no[m, i] + j
                            if e >= ST:
                                pe.wait_ge(s["prob_ready"], e - ST + 1)
                            mm = pe.matmul(ps[:, e % ST, q0:CW], k_op[a][j][:, TW * i:TW * i + TW],
                                           q_max[m % 2][:, q0:CW], start=True, stop=True)
                            if mask is not None:
                                width = mask.stop - mask.start
                                mm = pe.matmul(ps[:, e % ST, q0:q0 + width], k["identb"][:, :], k["mask_k"][:, mask],
                                               start=False, stop=True, skip_group_check=True)
                            mm.then_inc(s["st_filled"], 1)

                    def sum_values(b):
                        m, half = batches[b]
                        a = m // NC % 2
                        if m == NC and half == 0:
                            pe.wait_ge(s["v_ready"], 1)
                        if half == 0 and m > 0:
                            pe.wait_ge(s["sums_ready"], m)
                        pe.wait_ge(s["prob_ready"], 4 * (b + 1))
                        for kt in (2 * half, 2 * half + 1):
                            q0, _ = plan.first_query(m, kt)
                            for j in range(2):
                                g = 2 * (kt % 2) + j
                                e = 2 * exp_no[m, kt] + j
                                mm = pe.matmul(ps[VC * g:VC * g + VC, SUM, q0:CW], v_op[a][:, kt, j, :],
                                               prob[:, e % NP, q0:CW], start=(half == 0), stop=True,
                                               skip_group_check=True)
                        mm.then_inc(s["pv_done"], 1)

                    for kind, m, i in order:
                        if kind == "fill":
                            fill(m, i)
                        elif kind == "max":
                            turn_max(m)
                        else:
                            scores(m, i)
                            b = batch_no[m, i // 2]
                            if i % 2 == 1 and b >= 1:
                                sum_values(b - 1)
                    if exps:
                        sum_values(len(batches) - 1)

                @block.scalar
                def _(act):
                    def keep_sums(m):
                        act.wait_ge(s["pv_done"], last_batch(m) + 1)
                        if m >= 2:
                            act.wait_ge(s[f"sums_sent{m % 2}"], 16 * 8 * (m // 2))
                        nc.scalar.activation(sums[:, m % 2, :], ps[:, SUM, :], ACT.Copy).then_inc(s["sums_ready"], 1)

                    for _, m, i in exps:
                        q0, _ = plan.first_query(m, i)
                        for j in range(2):
                            e = 2 * exp_no[m, i] + j
                            act.wait_ge(s["st_filled"], e + 1)
                            if e >= NP and e % 4 == 0:
                                act.wait_ge(s["pv_done"], (e - NP) // 4 + 1)
                            nc.scalar.activation(prob[:, e % NP, q0:CW], ps[:, e % ST, q0:CW], ACT.Exp, scale=SCALE)\
                                .then_inc(s["prob_ready"], 1)
                        if i == 2 and m > 0:
                            keep_sums(m - 1)
                    if exps:
                        keep_sums(RING - 1)

                @block.vector
                def _(dve):
                    own = 0
                    for o in uses:
                        kind, m, f = o
                        u = use_no[o]
                        dve.wait_ge(s["mx_filled"], u + 1)
                        if kind == "max":
                            a, c = m // NC % 2, m % NC
                            if exps and m >= 2:
                                seen = [e for (mm, _), e in exp_no.items() if mm == m - 2]
                                dve.wait_ge(s["st_filled"], 2 * (max(seen) + 1))
                            nc.vector.tensor_tensor(q_max[m % 2][:, :], ps[:, MX + 2 * (u % 2), :],
                                                    chunk(q_op[a], c), ALU.add).then_inc(s["mx_used"], 1)
                            dve.wait_ge(s["mx_used"], u + 1)
                            dve.sem_inc(s["q_ready"], 1)
                            continue
                        qt, kc, w = plan.fills(m)[f]
                        nc.vector.tensor_reduce(blockmax[m % 2][:, qt, :, kc],
                                                ps[:, MX + 2 * (u % 2):MX + 2 * (u % 2) + 2, 0:w], AX.X, ALU.max)\
                            .then_inc(s["mx_used"], 1)
                        if f == len(plan.fills(m)) - 1:
                            dve.wait_ge(s["mx_used"], u + 1)
                            if max_no[m] > 0:
                                dve.wait_ge(s["max_split"], 4 * max_no[m])
                            nb = m % NC + 1 if plan.causal else NC
                            nc.vector.tensor_reduce(negmax[:, :, :], blockmax[m % 2][:, :, :, 0:nb], AX.X, ALU.max,
                                                    negate=True).then_inc(s["max_ready"], 1)

                @block.gpsimd
                def _(pool):
                    rows = maxparts[:, :, :].rearrange("p q (j r) -> p q j r", j=2)
                    hi, mid, lo = (rows[:, :, :, MAXROW + p] for p in range(3))

                    def take_values(a, col):
                        pool.tensor_copy(v_op[a][:, :, :, 0:HD],
                                         v_all[:, :, bass.ds(col, 2 * HD)].rearrange("p t (j d) -> p t j d", d=HD))\
                            .then_inc(s["v_ready"], 1)

                    if turn is not None:
                        take_values(1, turn * (4 * HD) + 2 * HD)
                    for _, m, _ in maxes:
                        t = 4 * max_no[m]
                        pool.wait_ge(s["max_ready"], max_no[m] + 1)
                        if max_no[m] > 0:
                            pool.wait_ge(s["mx_filled"], use_no["max", m - 1, 0] + 1)
                        pool.tensor_copy(hi, negmax[:, :, :]).then_inc(s["max_split"], 1)
                        pool.wait_ge(s["max_split"], t + 1)
                        pool.tensor_tensor(maxrest[:, :, :], negmax[:, :, :], hi, ALU.subtract)\
                            .then_inc(s["max_split"], 1)
                        pool.wait_ge(s["max_split"], t + 2)
                        pool.tensor_copy(mid, maxrest[:, :, :]).then_inc(s["max_split"], 1)
                        pool.wait_ge(s["max_split"], t + 3)
                        pool.tensor_tensor(lo, maxrest[:, :, :], mid, ALU.subtract).then_inc(s["max_split"], 1)
                        if turn is not None and m == NC + 1:
                            pool.wait_ge(s["pv_done"], last_batch(NC - 1) + 1)
                            take_values(0, turn * (4 * HD) + 4 * HD)

                if turn is not None:
                    @block.sync
                    def _(sp):
                        def send_sums(m):
                            head = turn * 4 + 2 * (m // NC)
                            sp.wait_ge(s["sums_ready"], m + 1)
                            pv_dram, p_dram = sums_dram
                            cols = slice(CW * (m % NC), CW * (m % NC) + CW)
                            for g in range(4):
                                sp.dma_start(pv_dram[g // 2, bass.ds(HD * (head + g % 2), HD), cols],
                                             sums[VC * g:VC * g + HD, m % 2, :]).then_inc(s[f"sums_sent{m % 2}"], 16)
                                sp.dma_start(p_dram[g // 2, bass.ds(head + g % 2, 1), cols],
                                             sums[VC * g + HD:VC * g + HD + 1, m % 2, :])\
                                    .then_inc(s[f"sums_sent{m % 2}"], 16)

                        load_pair(sp, 1, turn * (4 * HD) + 2 * HD)
                        for m in range(RING):
                            if m == NC:
                                sp.wait_ge(s["st_filled"], 2 * (exp_no[NC - 1, plan.keys(NC - 1) - 1] + 1))
                                load_pair(sp, 0, turn * (4 * HD) + 4 * HD)
                            send_sums(m)
                        for a in range(2):
                            sp.wait_ge(s[f"sums_sent{a}"], 16 * 8 * RING // 2)
                        sp.wait_ge(s["q_in0"], LOADED)
                        sp.wait_ge(s["k_in0"], LOADED)

        run(plan.before, None)
        nc.all_engine_barrier(sems_to_clear=loop_sems)
        with nc.Fori(0, PAIRS // 2) as turn:
            run(plan.turn, turn)
            nc.all_engine_barrier(sems_to_clear=loop_sems)


def project_out(nc, prefix, ps, k, xn, x, wproj, bproj, causal, sums_dram):
    with ExitStack() as stack:
        n = Names(nc, stack, prefix, k["banks"])
        num = [n.sb(f"num{a}", [P, N], fp32) for a in range(2)]
        den = [n.sb(f"den{a}", [P, N // SUB], fp32) for a in range(2)]
        num_in, den_in, den_sum, inverted = n.sem("num_in"), n.sem("den_in"), n.sem("den_sum"), n.sem("inverted")
        summed, spread, normed, projected = n.sem("summed"), n.sem("spread"), n.sem("normed"), n.sem("projected")
        pv_dram, p_dram = sums_dram
        DW = N // SUB
        with nc.Block() as block:
            @block.sync
            def _(sp):
                k["banks"].clear_last(sp)
                for a in range(2):
                    sp.dma_start(den[a][:, :], p_dram[a].rearrange("h (s t) -> (h s) t", s=SUB)).then_inc(den_in, 16)
                for a in range(2):
                    sp.dma_start(num[a][:, :], pv_dram[a]).then_inc(num_in, 16)

            @block.vector
            def _(dve):
                dve.wait_ge(den_in, 16 * 2)
                nc.vector.tensor_tensor(den[0][:, :], den[0][:, :], den[1][:, :], ALU.add).then_inc(den_sum, 1)
                dve.wait_ge(den_sum, 1)
                nc.vector.reciprocal(den[0][:, :], den[0][:, :]).then_inc(inverted, 1)
                dve.wait_ge(num_in, 16 * 2)
                for c in range(NC):
                    nc.vector.tensor_tensor(chunk(num[0], c), chunk(num[0], c), chunk(num[1], c), ALU.add)\
                        .then_inc(summed, 1)
                for c in range(NC):
                    dve.wait_ge(summed, c + 1)
                    dve.wait_ge(spread, c + 1)
                    nc.vector.tensor_tensor(chunk(num[0], c), chunk(num[0], c), ps[:, c, :], ALU.mult)\
                        .then_inc(normed, 1)
                for c in range(NC):
                    dve.wait_ge(projected, c + 1)
                    into = xn if causal else x
                    nc.vector.scalar_tensor_tensor(out=chunk(into, c), in0=ps[:, NC + c, :], scalar=bproj,
                                                   in1=chunk(into, c), op0=ALU.add, op1=ALU.add)

            @block.tensor
            def _(pe):
                pe.wait_ge(inverted, 1)
                for c in range(NC):
                    for t in range(CW // DW):
                        sub = CW // DW * c + t
                        mm = pe.matmul(ps[:, c, DW * t:DW * t + DW],
                                       k["spread"][:, sub, :, :].rearrange("p h d -> p (h d)"), den[0][:, :],
                                       start=True, stop=True)
                    mm.then_inc(spread, 1)
                for c in range(NC):
                    pe.wait_ge(normed, c + 1)
                    pe.matmul(ps[:, NC + c, :], wproj, chunk(num[0], c), start=True, stop=True).then_inc(projected, 1)


def macaron(nc, dram, out, stages="ABCDEF"):
    with ExitStack() as stack:
        n = Names(nc, stack, "m")
        ps = stack.enter_context(nc.psum_tensor("ps", [P, 8, CW], fp32))
        k = {"x": n.sb("x", [P, N], fp32)}
        x = k["x"]
        xn = n.sb("xn", [P, N], fp32)
        k["cen"], k["sq"] = n.sb("cen", [P, N], fp32), n.sb("sq", [P, N], fp32)
        k["std"], k["rstd"] = n.sb("std", [P, CW], fp32), n.sb("rstd", [P, CW], fp32)
        k["turn_sems"] = {name: n.sem(name) for name in TURN_SEMS}
        first, last = (k["turn_sems"][TURN_SEMS[i]].num for i in (0, -1))
        k["turn_sem_range"] = range(first, last + 1)
        assert len(k["turn_sem_range"]) == len(TURN_SEMS)
        k["banks"] = SemBanks(nc, stack)
        load_constants(nc, stack, ps, dram, k)

        def block_ffn(letter, ffn):
            layernorm(nc, letter + "n", ps, k, x, xn)
            ffn(nc, letter + "f", ps, k, xn, x)

        if "A" in stages:
            block_ffn("a", coupled_ffn)
        if "B" in stages:
            layernorm(nc, "bn", ps, k, x, xn)
            attention(nc, "ba", ps, k, xn, x, k["wqkv0"], k["wproj0"][:, :], k["bproj0"][:, 0:1], True, False)
            layernorm(nc, "bm", ps, k, xn, None, k["gamma"][:, 0:1], k["beta"][:, 0:1], add_to=x)
        if "C" in stages:
            block_ffn("c", coupled_ffn)
        if "D" in stages:
            block_ffn("d", moe_ffn)
        if "E" in stages:
            layernorm(nc, "en", ps, k, x, xn)
            attention(nc, "ea", ps, k, xn, x, k["wqkv1"], k["wproj1"][:, :], k["bproj1"][:, 0:1], False, True)
        if "F" in stages:
            block_ffn("f", moe_ffn)
        stored = n.sem("stored")
        with nc.Block() as block:
            @block.sync
            def _(sp):
                sp.dma_start(out, x[:, :]).then_inc(stored, 16)
                sp.wait_ge(stored, 16)


def layout(inputs):
    f = {name: np.asarray(a) for name, a in inputs.items()}
    col = lambda name, times=1: np.tile(f[name].reshape(-1, 1), (times, 1))
    z = {"x": f["L0_attn_target"][0].T}
    for i in (1, 2):
        z[f"cn_w{i}"] = f[f"L0_ffn_cn_w{i}"]
        z[f"gc_w{i}"] = f[f"L0_ffn_gc_w{i}"]
        z[f"gc_b{i}"] = col(f"L0_ffn_gc_b{i}")
    z["cn_w3"] = np.tile(f["L0_ffn_cn_w3"], (2, 1))
    z["cn_w4"] = np.tile(f["L0_ffn_cn_w4"], (4, P))
    z["gc_w3"] = np.tile(f["L0_ffn_gc_w3"], (1, P))
    z["cn_b1"], z["cn_b2"], z["cn_b3"] = col("L0_ffn_cn_b1"), col("L0_ffn_cn_b2", 2), col("L0_ffn_cn_b3", 4)
    z["cn_b4"], z["gc_b3"] = col("L0_ffn_cn_b4", P), col("L0_ffn_gc_b3", P)
    z["arange"] = col("L0_ffn_adaptive_range", P)
    z["wqkv0"], z["wproj0"], z["bproj0"] = f["L0_attn_w_qkv"], f["L0_attn_w_proj"], col("L0_attn_b_proj")
    z["gamma"], z["beta"] = col("L0_attn_ln_gamma"), col("L0_attn_ln_beta")
    z["wqkv1"], z["wproj1"], z["bproj1"] = f["L1_attn_w_qkv"], f["L1_attn_w_proj"], col("L1_attn_b_proj")
    z["wqT1"], z["wvT1"] = f["L1_attn_w_qkv"][:, 0:P].T, f["L1_attn_w_qkv"][:, 2 * P:].T
    for i, name in enumerate(("bq1", "bk1", "bv1")):
        z[name] = f["L1_attn_b_qkv"][P * i:P * i + P].reshape(-1, 1)
    for name, a, b in (("q", "L1_attn_a_q", "L1_attn_b_q"), ("v", "L1_attn_a_v", "L1_attn_b_v")):
        at = np.zeros((HEADS, LORA_R, HEADS, HD), np.float32)
        bm = np.zeros((HEADS, LORA_R, HEADS, HD), np.float32)
        for h in range(HEADS):
            at[h, :, h, :] = f[a].T
            bm[h, :, h, :] = f[b]
        z[f"a{name}T"] = at.reshape(2, P, P).transpose(1, 0, 2)
        z[f"b{name}"] = bm.reshape(2, P, P).transpose(1, 0, 2)
    z["router"] = f["L1_ffn_router"]
    z["e_gate"], z["e_up"], z["e_down"] = f["L1_ffn_experts_gate"], f["L1_ffn_experts_up"], f["L1_ffn_experts_down"]
    z["s_gate"], z["s_up"], z["s_down"] = f["L1_ffn_shared_gate"], f["L1_ffn_shared_up"], f["L1_ffn_shared_down"]
    return {name: np.ascontiguousarray(a) for name, a in z.items()}


STAGES = "ABCDEF"


def kernel(**inputs):
    import concourse.bacc as bacc
    from concourse.bass_utils import run_bass_kernel_spmd

    nc = bacc.Bacc("TRN2", target_bir_lowering=False, num_devices=1)
    arrays = layout(inputs)
    dram = {name: nc.dram_tensor(f"in_{name}", a.shape, mybir.dt.from_np(a.dtype), kind="ExternalInput").ap()
            for name, a in arrays.items()}
    out = nc.dram_tensor("out_x", (P, N), fp32, kind="ExternalOutput").ap()
    macaron(nc, dram, out, STAGES)
    r = run_bass_kernel_spmd(nc, [{f"in_{name}": a for name, a in arrays.items()}], core_ids=[0])
    return np.ascontiguousarray(r.results[0]["out_x"].T)[None]
```
